# Optimizing a Trainium2 kernel written in Bass

```python
import numpy as np
import jax
import jax.numpy as jnp

def _softmax(x, axis=-1):
    return jax.nn.softmax(x, axis=axis)

def _gelu(x):
    return jax.nn.gelu(x, approximate=True)

def _silu(x):
    return jax.nn.silu(x)

def _sigmoid(x):
    return jax.nn.sigmoid(x)

def _layernorm(x, axis=-1, eps=1e-05):
    m = jnp.mean(x, axis=axis, keepdims=True)
    v = jnp.var(x, axis=axis, keepdims=True)
    return (x - m) / jnp.sqrt(v + eps)

def _scatter_add(tgt, idx, src, axis=0):
    return tgt.at[idx].add(src)

def _segment_sum(src, seg, n):
    return jax.ops.segment_sum(src, seg, n)
kernel_name = 'mk_rec_standalone_d1_rec_r8_7e6605'

def setup_inputs(seed: int=0):
    np.random.seed(seed)
    _w = jnp.asarray

    def _rec_inputs():
        import jax
        import jax.numpy as jnp
        _rk = jax.random.key(seed)
        r_emb_inputs = 7.22013e-05 + 1.00017 * jax.random.normal(jax.random.fold_in(_rk, 1), (2048, 16, 256), jnp.float32)
        return r_emb_inputs
    r_emb_inputs = _rec_inputs()

    def _L0_rec_setup():
        import jax, jax.numpy as jnp
        import numpy as np
        NUM_FIELDS = 16
        EMBED = 256
        BATCH = 256
        NUM_PAIRS = NUM_FIELDS * (NUM_FIELDS - 1) // 2
        key = jax.random.key(seed)
        k1, k2, k3 = jax.random.split(key, 3)
        emb_inputs = jax.random.normal(k1, (BATCH, NUM_FIELDS, EMBED), dtype=jnp.float32)
        bound = 1.0 / np.sqrt(NUM_PAIRS)
        weight = jax.random.uniform(k2, (NUM_PAIRS, EMBED, EMBED), dtype=jnp.float32, minval=-bound, maxval=bound)
        bias = jax.random.uniform(k3, (NUM_PAIRS, EMBED), dtype=jnp.float32, minval=-bound, maxval=bound)
        return {'emb_inputs': emb_inputs, 'weight': weight, 'bias': bias}
    _L0_rec_all = _L0_rec_setup()
    _L0_rec_in = {k: v for k, v in _L0_rec_all.items() if k in ('weight', 'bias')}
    del _L0_rec_all
    return {'r_emb_inputs': r_emb_inputs, 'L0_rec_weight': _L0_rec_in['weight'], 'L0_rec_bias': _L0_rec_in['bias']}

def reference(r_emb_inputs, L0_rec_weight, L0_rec_bias):
    import jax
    import jax.numpy as jnp

    def _L0_rec_ref(emb_inputs, weight, bias):
        import jax, jax.numpy as jnp
        import numpy as np
        NUM_FIELDS = 16
        EMBED = 256
        BATCH = 256
        NUM_PAIRS = NUM_FIELDS * (NUM_FIELDS - 1) // 2
        row_idx, col_idx = np.triu_indices(NUM_FIELDS, k=1)
        p = emb_inputs[:, row_idx]
        q = emb_inputs[:, col_idx]
        out = jnp.einsum('bpe,pef->bpf', p, weight) * q + bias
        return out
    y = _L0_rec_ref(r_emb_inputs, L0_rec_weight, L0_rec_bias)
    return y

_drawn_inputs = setup_inputs


def setup_inputs(seed=0):
    import zlib

    import numpy as np

    out = dict(_drawn_inputs(seed))
    spreads = {}
    factors = {}
    for name, (base, spread) in spreads.items():
        noise = np.random.default_rng([zlib.crc32(name.encode()), seed]).standard_normal(out[name].shape)
        drawn = base * np.exp(spread * noise) if base else spread * noise
        out[name] = jnp.asarray(drawn.astype(out[name].dtype))
    for name, factor in factors.items():
        out[name] = (out[name] * factor).astype(out[name].dtype)
    return out
```

```python
from contextlib import ExitStack, contextmanager
from typing import NamedTuple

import concourse.bass as bass
from concourse import mybir

F32 = mybir.dt.float32
F32R = mybir.dt.float32r
ALU = mybir.AluOpType

P = 128
FIELDS = 16
EMBED = 256
BATCH = 2048
PAIRS = FIELDS * (FIELDS - 1) // 2
BLOCKS = 2
TILES = BATCH // P // BLOCKS
STEP_TILES = 2
STEPS = TILES // STEP_TILES
POOL_STEPS = STEPS - 1
CHUNKS = EMBED // P
HI, LO = 0, 1
ROWS = FIELDS - 1
EVEN_GROUPS = (FIELDS - 2) // 2
LAST_K = EVEN_GROUPS
BLOCK_GROUPS = (LAST_K + 1) ** 2


class Group(NamedTuple):
    seq: object
    before: object
    pair: object
    j: object
    width: int
    parity: int
    row: object
    next_i: object
    first: bool
    last: bool


class Walk:

    def __init__(self, eng):
        self.eng = eng
        self.seq = eng.alloc_register("groups_so_far")
        self.before = eng.alloc_register("group_before")
        self.pair = eng.alloc_register("pairs_so_far")
        eng.reg_mov(self.seq, 0)
        eng.reg_mov(self.before, 0)

    def bounded(self, value, high):
        return self.eng.bass.s_assert_within(value, 0, high, skip_runtime_bounds_check_because="the loops' ranges bound it")

    def start_block(self):
        self.eng.reg_mov(self.pair, 0)

    def one(self, group, blk, k, i, g, width, first=False, last=False):
        seq = self.eng.snap(self.bounded(self.eng.snap(self.seq), BLOCKS * BLOCK_GROUPS - 1))
        pair = self.eng.snap(self.bounded(self.eng.snap(self.pair), PAIRS - width))
        j = FIELDS - 1 if width == 1 else self.bounded(2 * k + i + 1 + 2 * g, FIELDS - width)
        before = self.eng.snap(self.before)
        group(Group(seq, before, pair, j, width, i, ROWS * blk + 2 * k + i, 2 * k + i + 1, first, last))
        self.eng.reg_mov(self.before, self.seq)
        self.eng.reg_add(self.seq, self.seq, 1)
        self.eng.reg_add(self.pair, self.pair, width)

    def row_pair(self, blk, k, group):
        if isinstance(k, int) and k == LAST_K:
            self.one(group, blk, k, 0, None, 1, last=True)
            return
        for i in range(2):
            self.one(group, blk, k, i, 0, 2, first=True)
            if not (isinstance(k, int) and k == LAST_K - 1):
                with self.eng.Fori(1, EVEN_GROUPS - k) as g:
                    self.one(group, blk, k, i, g, 2)
            if i == 0:
                self.one(group, blk, k, i, None, 1)

    def block(self, blk, group):
        with self.eng.Fori(0, LAST_K - 1) as k:
            self.row_pair(blk, k, group)
        self.row_pair(blk, LAST_K - 1, group)
        self.row_pair(blk, LAST_K, group)


def interaction_kernel(nc: bass.Bass, x: bass.AP, weight: bass.AP, bias: bass.AP, out: bass.AP):
    assert x.shape == (BATCH, FIELDS, EMBED) and weight.shape == (PAIRS, EMBED, EMBED)
    assert bias.shape == (PAIRS, EMBED) and out.shape == (BATCH, PAIRS, EMBED)

    with ExitStack() as ctx:
        def sbuf(name, shape, dtype):
            return ctx.enter_context(nc.sbuf_tensor(name, shape, dtype))

        def sem(name):
            return ctx.enter_context(nc.semaphore(name))

        rows = sbuf("rows", [P, TILES, FIELDS * EMBED], F32)
        turned = sbuf("turned", [P, 2, TILES, 2, CHUNKS, P], F32R)
        unturned = sbuf("unturned", [P, 2, STEP_TILES, EMBED], F32)
        w_raw = sbuf("w_raw", [P, 2, CHUNKS, EMBED], F32)
        w_split = sbuf("w_split", [P, 2, 2, 2, CHUNKS, EMBED], F32R)
        bias_all = sbuf("bias_all", [P, 2, 2 * EMBED], F32)
        staged = sbuf("staged", [P, STEPS, STEP_TILES, 2 * EMBED], F32)
        begun = sbuf("begun", [P, 4 + STEPS, 2], F32)
        identity = sbuf("identity", [P, P], F32)
        slots = ctx.enter_context(nc.psum_tensor("slots", [P, STEPS, STEP_TILES, 2 * EMBED], F32))

        identity_zero = sem("identity_zero")
        identity_ready = sem("identity_ready")
        x_landed = sem("x_landed")
        w_landed = sem("w_landed")
        bias_landed = sem("bias_landed")
        w_hi_ready = sem("w_hi_ready")
        w_lo_ready = sem("w_lo_ready")
        unturned_ready = sem("unturned_ready")
        turned_psum = sem("turned_psum")
        turned_hi = sem("turned_hi")
        turned_lo = sem("turned_lo")
        matmul_done = sem("matmul_done")
        slot_drained = sem("slot_drained")
        bias_added = sem("bias_added")
        last_added = sem("last_added")
        stored = [sem(f"stored_{s}") for s in range(STEPS)]

        x_cols = x.rearrange("(t p) n f -> p t (n f)", p=P)
        out_cols = out.rearrange("(t p) n f -> p t (n f)", p=P)
        w_rows = weight.rearrange("n (p c) f -> p n (c f)", c=CHUNKS)

        def biases_of(g):
            cols = g.width * EMBED
            return bias_all[:, bass.ds(g.seq % 2, 1), 0:cols].to_broadcast([P, STEP_TILES, cols])

        def step_tiles(s):
            return slice(STEP_TILES * s, STEP_TILES * (s + 1))

        def turning_slot(s):
            return (s + 2) % STEPS

        block = ctx.enter_context(nc.Block())

        @block.sync
        def _(sp):
            def load_fields(blk, m):
                if not (isinstance(m, int) and blk == 0 and m == 0):
                    sp.wait_ge(x_landed, 16 * (FIELDS // 2 * blk + m))
                sp.dma_start(rows[:, :, bass.ds(2 * EMBED * m, 2 * EMBED)],
                             x_cols[:, blk * TILES:(blk + 1) * TILES, bass.ds(2 * EMBED * m, 2 * EMBED)]
                             ).then_inc(x_landed, 16)

            earlier_bias_loads = sp.alloc_register("earlier_bias_loads")
            last_adds = sp.alloc_register("last_adds")

            def load_group(g, start=False):
                sp.reg_mov(earlier_bias_loads, 16 * g.seq)
                sp.reg_mov(last_adds, 1 + g.before)
                if not start:
                    sp.wait_ge(w_lo_ready, g.seq)
                sp.dma_start(w_raw[:, 0:g.width].rearrange("p n c f -> p n (c f)"),
                             w_rows[:, bass.ds(g.pair, g.width), :]).then_inc(w_landed, 16)
                if start:
                    load_fields(0, 0)
                else:
                    sp.wait_ge(bias_added, POOL_STEPS + POOL_STEPS * g.before)
                    sp.wait_ge(last_added, last_adds)
                    sp.wait_ge(bias_landed, earlier_bias_loads)
                sp.dma_start(bias_all[:, bass.ds(g.seq % 2, 1), 0:g.width * EMBED],
                             bias[bass.ds(g.pair, g.width), :].rearrange("n f -> (n f)")
                             .unsqueeze(0).partition_broadcast(P)
                             ).then_inc(bias_landed, 16)

            def first_row_group(g):
                start = g.parity == 0 and g.first
                load_group(g, start)
                if g.parity == 0 and g.width == 2:
                    load_fields(0, 1 if start else walk.bounded((g.j + 1) // 2, FIELDS // 2 - 1))

            def row_pair_of_block_0(k):
                def load(g):
                    load_group(g)
                    if g.parity == 1 and g.first:
                        sp.wait_ge(slot_drained, STEPS * g.before)
                        load_fields(1, k - 1)
                walk.row_pair(0, k, load)

            def next_block_group(g):
                load_group(g)
                if g.parity == 0 and g.first:
                    sp.wait_ge(slot_drained, STEPS + STEPS * BLOCK_GROUPS)
                    load_fields(1, LAST_K - 1)
                    load_fields(1, LAST_K)

            walk = Walk(sp)
            walk.start_block()
            walk.row_pair(0, 0, first_row_group)
            with sp.Fori(1, LAST_K - 1) as k:
                row_pair_of_block_0(k)
            row_pair_of_block_0(LAST_K - 1)
            walk.row_pair(0, LAST_K, load_group)
            walk.start_block()
            walk.row_pair(1, 0, next_block_group)
            with sp.Fori(1, LAST_K - 1) as k:
                walk.row_pair(1, k, load_group)
            walk.row_pair(1, LAST_K - 1, load_group)
            walk.row_pair(1, LAST_K, load_group)

        @block.tensor
        def _(pe):
            def turn(row, s, parity):
                pe.wait_ge(unturned_ready, STEPS * row + s + 1)
                for t in range(STEP_TILES):
                    for c in range(CHUNKS):
                        at = P * (CHUNKS * t + c)
                        mm = pe.transpose(slots[:, turning_slot(s), 0, at:at + P],
                                          unturned[:, s % 2, t, c::CHUNKS], identity[:, :])
                mm.then_inc(turned_psum, 1)

            def group(g):
                cols = g.width * EMBED
                pe.wait_ge(w_hi_ready, g.seq + 1)
                pe.wait_ge(w_lo_ready, g.seq + 1)
                weights = w_split[:, bass.ds(g.seq % 2, 1)]

                for s in range(STEPS):
                    pe.wait_ge(slot_drained, STEPS * g.seq + s + 1)
                    turnings = STEPS * (g.row if g.first or g.last else g.row + 1)
                    turnings = turnings + turning_slot(s) + 1 if s < 2 else None
                    if g.first and s >= 2:
                        turnings = STEPS * (g.row + 1) + s - 1
                    if turnings is not None:
                        pe.wait_ge(turned_hi, turnings)
                        pe.wait_ge(turned_lo, turnings)
                    for t in range(STEP_TILES):
                        sums = slots[:, s, t, 0:cols]
                        for c in range(CHUNKS):
                            for part, parts in ((HI, (HI, LO)), (LO, (HI,))):
                                p = turned[:, g.parity, STEP_TILES * s + t, part, c, :]
                                for w in parts:
                                    mm = pe.matmul(sums, p,
                                                   weights[:, :, w, 0:g.width, c, :].rearrange("p o n f -> p (o n) f"),
                                                   start=(c == 0 and part == HI and w == HI),
                                                   stop=(c == CHUNKS - 1 and part == LO))
                    mm.then_inc(matmul_done, 1)
                    if g.first:
                        pe.wait_ge(slot_drained, STEPS * g.seq + s + 3)
                        turn(g.row + 1, s, 1 - g.parity)

            pe.wait_ge(identity_ready, 1)
            walk = Walk(pe)
            with pe.Fori(0, BLOCKS) as blk:
                walk.start_block()
                pe.wait_ge(slot_drained, STEPS + STEPS * BLOCK_GROUPS * blk)
                for s in range(STEPS):
                    turn(ROWS * blk, s, 0)
                walk.block(blk, group)

        @block.scalar
        def _(act):
            def split_turned(row, s, parity):
                act.wait_ge(turned_psum, STEPS * row + s + 1)
                nc.scalar.copy(turned[:, parity, step_tiles(s), HI].rearrange("p t c b -> p t (c b)"),
                               slots[:, turning_slot(s), 0, :].rearrange("p (t e) -> p t e", t=STEP_TILES)
                               ).then_inc(turned_hi, 1)

            def split_weights(seq, done):
                act.wait_ge(w_landed, 16 * (seq + 1))
                act.wait_ge(matmul_done, done)
                nc.scalar.copy(w_split[:, bass.ds(seq % 2, 1), HI].rearrange("p o n c f -> p (o n c f)"),
                               w_raw[:].rearrange("p n c f -> p (n c f)")).then_inc(w_hi_ready, 1)

            def store(blk, g, s):
                if s < POOL_STEPS:
                    act.wait_ge(bias_added, POOL_STEPS + POOL_STEPS * g.seq + s + 1)
                else:
                    act.wait_ge(last_added, 1 + g.seq + 1)
                act.dma_start(out_cols[:, bass.ds(blk * TILES + STEP_TILES * s, STEP_TILES),
                                       bass.ds(g.pair * EMBED, g.width * EMBED)],
                              staged[:, s, :, 0:g.width * EMBED]).then_inc(stored[s], 16)

            walk = Walk(act)
            with act.Fori(0, BLOCKS) as blk:
                walk.start_block()
                def group(g):
                    if g.first:
                        split_turned(g.row + 1, 0, 1 - g.parity)
                    if not g.last:
                        split_weights(g.seq + 1, STEPS + STEPS * g.seq)
                    for s in range(STEPS):
                        if g.first and s < STEPS - 1:
                            split_turned(g.row + 1, s + 1, 1 - g.parity)
                        store(blk, g, s)

                for s in range(STEPS):
                    split_turned(ROWS * blk, s, 0)
                split_weights(BLOCK_GROUPS * blk, STEPS + STEPS * BLOCK_GROUPS * blk)
                walk.block(blk, group)
            for s in range(STEPS):
                act.wait_ge(stored[s], 16 + 16 * BLOCKS * BLOCK_GROUPS)

        @block.vector
        def _(dve):
            def fetch(i, s):
                nc.vector.tensor_copy(unturned[:, s % 2], rows[:, step_tiles(s), bass.ds(i * EMBED, EMBED)]
                                      ).then_inc(unturned_ready, 1)

            def split_turned(row, s, parity):
                dve.wait_ge(turned_hi, STEPS * row + s + 1)
                high = turned[:, parity, step_tiles(s), HI].rearrange("p t c b -> p t (c b)")
                nc.vector.tensor_tensor(turned[:, parity, step_tiles(s), LO].rearrange("p t c b -> p t (c b)"),
                                        slots[:, turning_slot(s), 0, :].rearrange("p (t e) -> p t e", t=STEP_TILES),
                                        high.bitcast(F32), ALU.subtract).then_inc(turned_lo, 1)

            def split_weights(seq):
                dve.wait_ge(w_hi_ready, seq + 1)
                half = w_split[:, bass.ds(seq % 2, 1)]
                nc.vector.tensor_tensor(half[:, :, LO].rearrange("p o n c f -> p (o n c f)"),
                                        w_raw[:].rearrange("p n c f -> p (n c f)"),
                                        half[:, :, HI].rearrange("p o n c f -> p (o n c f)").bitcast(F32),
                                        ALU.subtract).then_inc(w_lo_ready, 1)

            counts = [(slot_drained, STEPS), (matmul_done, STEPS), (bias_added, POOL_STEPS), (last_added, 1)]
            for n, (count, value) in enumerate(counts + [(x, 16) for x in stored]):
                nc.vector.memset(begun[:, n], 0.0).then_inc(count, value)
            walk = Walk(dve)
            with dve.Fori(0, BLOCKS) as blk:
                walk.start_block()
                def group(g):
                    cols = g.width * EMBED
                    if g.first:
                        fetch(g.next_i, 0)
                        fetch(g.next_i, 1)
                    dve.wait_ge(x_landed, 16 * (FIELDS // 2 * blk + (g.j + g.width - 1) // 2 + 1))
                    for s in range(STEPS):
                        dve.wait_ge(matmul_done, STEPS + STEPS * g.seq + s + 1)
                        dve.wait_ge(stored[s], 16 + 16 * g.seq)
                        nc.vector.tensor_tensor(staged[:, s, :, 0:cols], slots[:, s, :, 0:cols],
                                                rows[:, step_tiles(s), bass.ds(g.j * EMBED, cols)],
                                                ALU.mult).then_inc(slot_drained, 1)
                        if g.first:
                            split_turned(g.row + 1, s, 1 - g.parity)
                            if s + 2 < STEPS:
                                fetch(g.next_i, s + 2)
                        if s == 1 and not g.last:
                            split_weights(g.seq + 1)
                    dve.wait_ge(bias_landed, 16 * (g.seq + 1))
                    dve.wait_ge(slot_drained, STEPS + STEPS * g.seq + STEPS)
                    values = staged[:, STEPS - 1, :, 0:cols]
                    nc.vector.tensor_tensor(values, values, biases_of(g), ALU.add).then_inc(last_added, 1)

                dve.wait_ge(x_landed, 16 * (FIELDS // 2 * blk + 1))
                fetch(0, 0)
                fetch(0, 1)
                for s in range(STEPS):
                    split_turned(ROWS * blk, s, 0)
                    if s + 2 < STEPS:
                        fetch(0, s + 2)
                split_weights(BLOCK_GROUPS * blk)
                walk.block(blk, group)

        @block.gpsimd
        def _(pool):
            nc.gpsimd.memset(identity[:], 0.0).then_inc(identity_zero, 1)
            pool.wait_ge(identity_zero, 1)
            nc.gpsimd.affine_select(out=identity[:], in_=identity[:], compare_op=ALU.not_equal, fill=1.0,
                                    base=0, pattern=[[-1, P]], channel_multiplier=1).then_inc(identity_ready, 1)

            products = [pool.alloc_register(f"products_{n}") for n in range(POOL_STEPS)]
            pool.reg_mov(products[0], STEPS + 1)

            def group(g):
                cols = g.width * EMBED
                biases = biases_of(g)
                pool.wait_ge(bias_landed, 16 * (g.seq + 1))
                for s in range(POOL_STEPS):
                    pool.wait_ge(slot_drained, products[s])
                    skip = STEPS - POOL_STEPS if s == POOL_STEPS - 1 else 0
                    pool.reg_add(products[(s + 1) % POOL_STEPS], products[s], 1 + skip)
                    nc.gpsimd.tensor_tensor(staged[:, s, :, 0:cols], staged[:, s, :, 0:cols], biases,
                                            ALU.add).then_inc(bias_added, 1)

            walk = Walk(pool)
            with pool.Fori(0, BLOCKS) as blk:
                walk.start_block()
                walk.block(blk, group)


def kernel(r_emb_inputs, L0_rec_weight, L0_rec_bias):
    import numpy as np
    import concourse.bacc as bacc
    from concourse.bass_utils import run_bass_kernel_spmd

    nc = bacc.Bacc("TRN2", target_bir_lowering=False, num_devices=1)
    arrays, aps = {}, []
    for name, a in (("x", r_emb_inputs), ("weight", L0_rec_weight), ("bias", L0_rec_bias)):
        a = np.ascontiguousarray(a)
        arrays[name] = a
        aps.append(nc.dram_tensor(name, a.shape, F32, kind="ExternalInput").ap())
    out = nc.dram_tensor("out", (BATCH, PAIRS, EMBED), F32, kind="ExternalOutput").ap()
    interaction_kernel(nc, *aps, out)
    return run_bass_kernel_spmd(nc, [arrays], core_ids=[0]).results[0]["out"]
```
